# Optimizing a Trainium2 kernel written in Bass

```python
import numpy as np
import jax
import jax.numpy as jnp

def _softmax(x, axis=-1):
    return jax.nn.softmax(x, axis=axis)

def _gelu(x):
    return jax.nn.gelu(x, approximate=True)

def _silu(x):
    return jax.nn.silu(x)

def _sigmoid(x):
    return jax.nn.sigmoid(x)

def _layernorm(x, axis=-1, eps=1e-05):
    m = jnp.mean(x, axis=axis, keepdims=True)
    v = jnp.var(x, axis=axis, keepdims=True)
    return (x - m) / jnp.sqrt(v + eps)

def _scatter_add(tgt, idx, src, axis=0):
    return tgt.at[idx].add(src)

def _segment_sum(src, seg, n):
    return jax.ops.segment_sum(src, seg, n)
kernel_name = 'mk_dlrm_tower_d1_rec_r8_39d510'

def setup_inputs(seed: int=0):
    np.random.seed(seed)
    _w = jnp.asarray

    def _rec_inputs():
        import jax
        import jax.numpy as jnp
        _tk = jax.random.key(seed)
        ids = jnp.stack([jax.random.randint(jax.random.fold_in(_tk, 200 + f), (512,), 0, v, jnp.int32) for f, v in enumerate([1250, 1000, 1000, 125000, 1250, 12500, 1250, 12500, 1250, 1250, 1250, 1250, 1000, 1000, 1000, 12500, 1250, 1250, 1000, 1000, 1250, 12500, 12500, 12500, 1000, 1000])], axis=1)
        tbl_0 = 0.05 * jax.random.normal(jax.random.fold_in(_tk, 500 + 0), (1250, 128), jnp.float32)
        tbl_1 = 0.05 * jax.random.normal(jax.random.fold_in(_tk, 500 + 1), (1000, 128), jnp.float32)
        tbl_2 = 0.05 * jax.random.normal(jax.random.fold_in(_tk, 500 + 2), (1000, 128), jnp.float32)
        tbl_3 = 0.05 * jax.random.normal(jax.random.fold_in(_tk, 500 + 3), (125000, 128), jnp.float32)
        tbl_4 = 0.05 * jax.random.normal(jax.random.fold_in(_tk, 500 + 4), (1250, 128), jnp.float32)
        tbl_5 = 0.05 * jax.random.normal(jax.random.fold_in(_tk, 500 + 5), (12500, 128), jnp.float32)
        tbl_6 = 0.05 * jax.random.normal(jax.random.fold_in(_tk, 500 + 6), (1250, 128), jnp.float32)
        tbl_7 = 0.05 * jax.random.normal(jax.random.fold_in(_tk, 500 + 7), (12500, 128), jnp.float32)
        tbl_8 = 0.05 * jax.random.normal(jax.random.fold_in(_tk, 500 + 8), (1250, 128), jnp.float32)
        tbl_9 = 0.05 * jax.random.normal(jax.random.fold_in(_tk, 500 + 9), (1250, 128), jnp.float32)
        tbl_10 = 0.05 * jax.random.normal(jax.random.fold_in(_tk, 500 + 10), (1250, 128), jnp.float32)
        tbl_11 = 0.05 * jax.random.normal(jax.random.fold_in(_tk, 500 + 11), (1250, 128), jnp.float32)
        tbl_12 = 0.05 * jax.random.normal(jax.random.fold_in(_tk, 500 + 12), (1000, 128), jnp.float32)
        tbl_13 = 0.05 * jax.random.normal(jax.random.fold_in(_tk, 500 + 13), (1000, 128), jnp.float32)
        tbl_14 = 0.05 * jax.random.normal(jax.random.fold_in(_tk, 500 + 14), (1000, 128), jnp.float32)
        tbl_15 = 0.05 * jax.random.normal(jax.random.fold_in(_tk, 500 + 15), (12500, 128), jnp.float32)
        tbl_16 = 0.05 * jax.random.normal(jax.random.fold_in(_tk, 500 + 16), (1250, 128), jnp.float32)
        tbl_17 = 0.05 * jax.random.normal(jax.random.fold_in(_tk, 500 + 17), (1250, 128), jnp.float32)
        tbl_18 = 0.05 * jax.random.normal(jax.random.fold_in(_tk, 500 + 18), (1000, 128), jnp.float32)
        tbl_19 = 0.05 * jax.random.normal(jax.random.fold_in(_tk, 500 + 19), (1000, 128), jnp.float32)
        tbl_20 = 0.05 * jax.random.normal(jax.random.fold_in(_tk, 500 + 20), (1250, 128), jnp.float32)
        tbl_21 = 0.05 * jax.random.normal(jax.random.fold_in(_tk, 500 + 21), (12500, 128), jnp.float32)
        tbl_22 = 0.05 * jax.random.normal(jax.random.fold_in(_tk, 500 + 22), (12500, 128), jnp.float32)
        tbl_23 = 0.05 * jax.random.normal(jax.random.fold_in(_tk, 500 + 23), (12500, 128), jnp.float32)
        tbl_24 = 0.05 * jax.random.normal(jax.random.fold_in(_tk, 500 + 24), (1000, 128), jnp.float32)
        tbl_25 = 0.05 * jax.random.normal(jax.random.fold_in(_tk, 500 + 25), (1000, 128), jnp.float32)
        _rk = jax.random.fold_in(_tk, 7)
        r_dense_features = -0.000520686 + 1.00062 * jax.random.normal(jax.random.fold_in(_rk, 101), (512, 128), jnp.float32)
        W_top1 = 0.0405887 * jax.random.normal(jax.random.fold_in(_tk, 801), (607, 512), jnp.float32)
        W_top2 = 0.0441942 * jax.random.normal(jax.random.fold_in(_tk, 802), (512, 256), jnp.float32)
        W_top3 = 0.0625 * jax.random.normal(jax.random.fold_in(_tk, 803), (256, 1), jnp.float32)
        b_top1 = jnp.zeros((512,), jnp.float32)
        b_top2 = jnp.zeros((256,), jnp.float32)
        return (r_dense_features, ids, tbl_0, tbl_1, tbl_2, tbl_3, tbl_4, tbl_5, tbl_6, tbl_7, tbl_8, tbl_9, tbl_10, tbl_11, tbl_12, tbl_13, tbl_14, tbl_15, tbl_16, tbl_17, tbl_18, tbl_19, tbl_20, tbl_21, tbl_22, tbl_23, tbl_24, tbl_25, W_top1, b_top1, W_top2, b_top2, W_top3)
    r_dense_features, ids, tbl_0, tbl_1, tbl_2, tbl_3, tbl_4, tbl_5, tbl_6, tbl_7, tbl_8, tbl_9, tbl_10, tbl_11, tbl_12, tbl_13, tbl_14, tbl_15, tbl_16, tbl_17, tbl_18, tbl_19, tbl_20, tbl_21, tbl_22, tbl_23, tbl_24, tbl_25, W_top1, b_top1, W_top2, b_top2, W_top3 = _rec_inputs()

    def _L0_rec_setup():
        import jax, jax.numpy as jnp
        import numpy as np
        NUM_SPARSE = 26
        EMBED_DIM = 128
        BATCH = 2048
        key = jax.random.key(seed)
        k1, k2 = jax.random.split(key)
        dense_features = jax.random.normal(k1, (BATCH, EMBED_DIM), dtype=jnp.float32)
        sparse_features = jax.random.normal(k2, (BATCH, NUM_SPARSE, EMBED_DIM), dtype=jnp.float32)
        return {'dense_features': dense_features, 'sparse_features': sparse_features}
    _L0_rec_all = _L0_rec_setup()
    _L0_rec_in = {k: v for k, v in _L0_rec_all.items() if k in ()}
    del _L0_rec_all
    return {'r_dense_features': r_dense_features, 'ids': ids, 'tbl_0': tbl_0, 'tbl_1': tbl_1, 'tbl_2': tbl_2, 'tbl_3': tbl_3, 'tbl_4': tbl_4, 'tbl_5': tbl_5, 'tbl_6': tbl_6, 'tbl_7': tbl_7, 'tbl_8': tbl_8, 'tbl_9': tbl_9, 'tbl_10': tbl_10, 'tbl_11': tbl_11, 'tbl_12': tbl_12, 'tbl_13': tbl_13, 'tbl_14': tbl_14, 'tbl_15': tbl_15, 'tbl_16': tbl_16, 'tbl_17': tbl_17, 'tbl_18': tbl_18, 'tbl_19': tbl_19, 'tbl_20': tbl_20, 'tbl_21': tbl_21, 'tbl_22': tbl_22, 'tbl_23': tbl_23, 'tbl_24': tbl_24, 'tbl_25': tbl_25, 'W_top1': W_top1, 'b_top1': b_top1, 'W_top2': W_top2, 'b_top2': b_top2, 'W_top3': W_top3}

def reference(r_dense_features, ids, tbl_0, tbl_1, tbl_2, tbl_3, tbl_4, tbl_5, tbl_6, tbl_7, tbl_8, tbl_9, tbl_10, tbl_11, tbl_12, tbl_13, tbl_14, tbl_15, tbl_16, tbl_17, tbl_18, tbl_19, tbl_20, tbl_21, tbl_22, tbl_23, tbl_24, tbl_25, W_top1, b_top1, W_top2, b_top2, W_top3):
    import jax
    import jax.numpy as jnp

    def _L0_rec_ref(dense_features, sparse_features):
        import jax, jax.numpy as jnp
        import numpy as np
        NUM_SPARSE = 26
        EMBED_DIM = 128
        BATCH = 2048
        F = NUM_SPARSE + 1
        combined = jnp.concatenate([dense_features[:, None, :], sparse_features], axis=1)
        interactions = jnp.einsum('bfd,bgd->bfg', combined, combined)
        iu, ju = jnp.triu_indices(F, k=1)
        interactions_flat = interactions[:, iu, ju]
        return jnp.concatenate([dense_features, interactions_flat], axis=1)
    e = jnp.stack([tbl_0[ids[:, 0]], tbl_1[ids[:, 1]], tbl_2[ids[:, 2]], tbl_3[ids[:, 3]], tbl_4[ids[:, 4]], tbl_5[ids[:, 5]], tbl_6[ids[:, 6]], tbl_7[ids[:, 7]], tbl_8[ids[:, 8]], tbl_9[ids[:, 9]], tbl_10[ids[:, 10]], tbl_11[ids[:, 11]], tbl_12[ids[:, 12]], tbl_13[ids[:, 13]], tbl_14[ids[:, 14]], tbl_15[ids[:, 15]], tbl_16[ids[:, 16]], tbl_17[ids[:, 17]], tbl_18[ids[:, 18]], tbl_19[ids[:, 19]], tbl_20[ids[:, 20]], tbl_21[ids[:, 21]], tbl_22[ids[:, 22]], tbl_23[ids[:, 23]], tbl_24[ids[:, 24]], tbl_25[ids[:, 25]]], axis=1)
    z = _L0_rec_ref(r_dense_features, e)
    z = z.reshape(z.shape[0], -1)
    h = jnp.concatenate([z, r_dense_features], axis=1)
    h = jnp.maximum(h @ W_top1 + b_top1, 0.0)
    h = jnp.maximum(h @ W_top2 + b_top2, 0.0)
    y = h @ W_top3
    return y

_drawn_inputs = setup_inputs


def setup_inputs(seed=0):
    import zlib

    import numpy as np

    out = dict(_drawn_inputs(seed))
    spreads = {'b_top1': (0.0, 0.1), 'b_top2': (0.0, 0.1)}
    factors = {}
    for name, (base, spread) in spreads.items():
        noise = np.random.default_rng([zlib.crc32(name.encode()), seed]).standard_normal(out[name].shape)
        drawn = base * np.exp(spread * noise) if base else spread * noise
        out[name] = jnp.asarray(drawn.astype(out[name].dtype))
    for name, factor in factors.items():
        out[name] = (out[name] * factor).astype(out[name].dtype)
    return out
```

```python
from contextlib import ExitStack

import concourse.bass as bass
from concourse import mybir

F32 = mybir.dt.float32
I32 = mybir.dt.int32
U32 = mybir.dt.uint32
ALU = mybir.AluOpType
ACT = mybir.ActivationFunctionType


def bass_dlrm_tower(nc, ids, dense, tables, w1_pairs, w1_dense, w2, params, out):
    P = 128
    B, D = dense.shape
    NT = len(tables)
    F = NT + 1
    TILES = B // P
    SLOT = 32
    NS = P // SLOT
    NQ = P // NS
    HALF = (F - 1) // 2
    KP = w1_pairs.shape[0]
    NKP = w1_pairs.shape[1]
    H1 = w1_pairs.shape[2]
    H2 = w2.shape[2]
    J1, J2 = H1 // P, H2 // P
    GF = 4
    groups = [list(range(a, min(a + GF, NT))) for a in range(0, NT, GF)]
    NG = len(groups)
    QC = 8
    NCH = NQ // QC
    QB = 4

    with ExitStack() as ctx:
        def sb(name, shape, dt=F32):
            return ctx.enter_context(nc.sbuf_tensor(name, shape, dt))

        def psum(name, shape):
            return ctx.enter_context(nc.psum_tensor(name, shape, F32))

        def sem(name):
            return ctx.enter_context(nc.semaphore(name))

        ids_sb = sb("ids_sb", [P, TILES, NT], I32)
        x_sb = sb("x_sb", [P, TILES, D])
        rows = sb("rows", [P, TILES, NT, D])
        ident = sb("ident", [P, P])
        featT = sb("featT", [P, TILES, NQ, NS, SLOT])
        xT = sb("xT", [P, TILES, P])
        gram = sb("gram", [P, 2, NQ, F])
        gramT = sb("gramT", [P, 2, F + HALF, SLOT])
        pairs = sb("pairs", [P, 2, F, HALF])
        pairsT = sb("pairsT", [P, 2, NKP, P])
        w1p_sb = sb("w1p_sb", [P, NKP, H1])
        w1d_sb = sb("w1d_sb", [P, 2, H1])
        w1x = sb("w1x", [P, H1])
        w2_sb = sb("w2_sb", [P, J1, H2])
        par_sb = sb("par_sb", [P, J1 + J2 + J2])
        h1T = sb("h1T", [P, 2, J1, P])
        h2T = sb("h2T", [P, 2, J2, P])
        y_sb = sb("y_sb", [1, P, TILES])

        tr_ps = psum("tr_ps", [P, 2, GF, P])
        gram_ps = psum("gram_ps", [P, 2, 2, 512])
        mix_ps = psum("mix_ps", [P, 512])
        h1_ps = psum("h1_ps", [P, 512])

        ids_in, x_in, w1p_in, w1d_in, w2_in, par_in = map(sem, (
            "ids_in", "x_in", "w1p_in", "w1d_in", "w2_in", "par_in"))
        rows_in = [[sem(f"rows_in_{t}_{g}") for g in range(NG)] for t in range(TILES)]
        ident_zero, ident_ready, pad_zero = sem("ident_zero"), sem("ident_ready"), sem("pad_zero")
        w1x_ready = sem("w1x_ready")
        tr_done = sem("tr_done")
        tr_act, tr_dve = sem("tr_act"), sem("tr_dve")
        gram_done = sem("gram_done")
        diag_act, diag_dve = sem("diag_act"), sem("diag_dve")
        gramT_ready, pairs_ready = sem("gramT_ready"), sem("pairs_ready")
        pairsT_done, pairsT_ready = sem("pairsT_done"), sem("pairsT_ready")
        h1_done, h1_ready = sem("h1_done"), sem("h1_ready")
        h2_done, h2_ready = sem("h2_done"), sem("h2_ready")
        y_done, y_ready, y_out = sem("y_done"), sem("y_ready"), sem("y_out")

        def turn(t, g):
            return 1 + t * NG + g

        def dve_turns(n):
            return n // 2 + 1

        def act_turns(n):
            return (n + 1) // 2

        block = ctx.enter_context(nc.Block())

        @block.sync
        def _(sp):
            sp.dma_start(ids_sb[:, :, :], ids.rearrange("(p t) f -> p t f", t=TILES)).then_inc(ids_in, 16)
            sp.dma_start(x_sb[:, :, :], dense.rearrange("(p t) d -> p t d", t=TILES)).then_inc(x_in, 16)
            sp.dma_start(par_sb[:, :], params).then_inc(par_in, 16)
            sp.dma_start(w1d_sb[:, :, :], w1_dense).then_inc(w1d_in, 16)
            sp.dma_start(w1p_sb[0:KP, :, :], w1_pairs).then_inc(w1p_in, 16)
            sp.dma_start(w2_sb[:, :, :], w2).then_inc(w2_in, 16)
            sp.wait_ge(y_ready, TILES)
            sp.dma_start(out.rearrange("(a p t) o -> a p (t o)", a=1, t=TILES), y_sb[:, :, :]).then_inc(y_out, 16)
            sp.wait_ge(y_out, 16)

        @block.gpsimd
        def _(pool):
            nc.gpsimd.memset(ident[:, :], 0.0).then_inc(ident_zero, 1)
            pool.wait_ge(ident_zero, 1)
            nc.gpsimd.affine_select(out=ident[:, :], in_=ident[:, :], compare_op=ALU.not_equal, fill=1.0,
                                    base=0, pattern=[[-1, P]], channel_multiplier=1).then_inc(ident_ready, 1)
            pool.wait_ge(ids_in, 16)
            for t in range(TILES):
                for g, fs in enumerate(groups):
                    for f in fs:
                        pool.indirect_dma_start(
                            out=rows[:, t, f, :], out_offset=None, in_=tables[f][:, :],
                            in_offset=bass.IndirectOffsetOnAxis(ap=ids_sb[:, t, f:f + 1].bitcast(U32), axis=0),
                        ).then_inc(rows_in[t][g], 16)

        def store_features(copy, t, g, n):
            fs = groups[g]
            src = tr_ps[:, n % 2, 0:len(fs), :].rearrange("d f (s q) -> d f s q", s=NS)
            dst = featT[:, t, :, :, 1 + fs[0]:2 + fs[-1]].rearrange("d q s f -> d f s q")
            last = None
            for s in range(NS):
                last = copy(dst[:, :, s, :], src[:, :, s, :])
            return last

        def store_diagonal(copy, t, c, s):
            src = gram_ps[SLOT * s:SLOT * (s + 1), (t * NCH + c) % 2, :, 0:QB * NS * F]
            src = src.rearrange("p b (q r g) -> p b q r g", q=QB, r=NS)[:, :, :, s, :]
            dst = gram[SLOT * s:SLOT * (s + 1), t % 2, c * QC:(c + 1) * QC, :]
            return copy(dst.rearrange("p (b q) g -> p b q g", q=QB), src)

        @block.scalar
        def _(act):
            def features(t, g):
                n = turn(t, g)
                act.wait_ge(tr_done, n + 1)
                store_features(nc.scalar.copy, t, g, n).then_inc(tr_act, 1)

            def diagonals(t, c):
                act.wait_ge(gram_done, t * NCH + c + 1)
                if c == 0 and t >= 2:
                    act.wait_ge(gramT_ready, t - 1)
                for s in (0, 1):
                    last = store_diagonal(nc.scalar.copy, t, c, s)
                last.then_inc(diag_act, 1)

            def hidden1(t):
                act.wait_ge(h1_done, t + 1)
                if t >= 2:
                    act.wait_ge(h2_done, t - 1)
                for j in range(J1):
                    last = nc.scalar.activation(h1T[:, t % 2, j, :], h1_ps[:, j * P:(j + 1) * P], ACT.Relu,
                                                bias=par_sb[:, j:j + 1])
                last.then_inc(h1_ready, 1)

            def hidden2(t):
                act.wait_ge(h2_done, t + 1)
                if t >= 2:
                    act.wait_ge(y_done, t - 1)
                for j in range(J2):
                    last = nc.scalar.activation(h2T[:, t % 2, j, :], mix_ps[:, j * P:(j + 1) * P], ACT.Relu,
                                                bias=par_sb[:, J1 + j:J1 + j + 1])
                last.then_inc(h2_ready, 1)

            def result(t):
                act.wait_ge(y_done, t + 1)
                nc.scalar.copy(y_sb[0:1, :, t], h1_ps[0:1, 0:P]).then_inc(y_ready, 1)

            act.wait_ge(tr_done, 1)
            act.wait_ge(tr_dve, 1)
            nc.scalar.copy(xT[:, :, :], tr_ps[:, 0, :, :]).then_inc(tr_act, 1)
            act.wait_ge(par_in, 16)
            for t in range(TILES):
                for g in range(NG):
                    if turn(t, g) % 2:
                        features(t, g)
                    if t >= 1:
                        if g == 2:
                            hidden1(t - 1)
                        if g == 3:
                            hidden2(t - 1)
                        if g == 4:
                            result(t - 1)
                for c in range(NCH):
                    diagonals(t, c)
            hidden1(TILES - 1)
            hidden2(TILES - 1)
            result(TILES - 1)

        @block.vector
        def _(dve):
            def features(t, g):
                n = turn(t, g)
                dve.wait_ge(tr_done, n + 1)
                store_features(nc.vector.tensor_copy, t, g, n).then_inc(tr_dve, 1)

            def diagonals(t, c):
                dve.wait_ge(gram_done, t * NCH + c + 1)
                for s in (2, 3):
                    last = store_diagonal(nc.vector.tensor_copy, t, c, s)
                last.then_inc(diag_dve, 1)

            def arrange_pairs(t):
                dve.wait_ge(diag_dve, NCH * (t + 1))
                dve.wait_ge(diag_act, NCH * (t + 1))
                src = gram[:, t % 2, :, :].rearrange("p q g -> p g q")
                nc.vector.transpose(gramT[:, t % 2, 0:F, :], src)
                nc.vector.transpose(gramT[:, t % 2, F:F + HALF, :], src[:, 0:HALF, :]).then_inc(gramT_ready, 1)
                dve.wait_ge(gramT_ready, t + 1)
                if t >= 2:
                    dve.wait_ge(pairsT_done, t - 1)
                flat = gramT[:, t % 2, :, :].rearrange("p g f -> p (g f)")
                diag = bass.AP(flat.tensor, flat.offset + SLOT, [list(flat.ap[0]), [SLOT + 1, F], [SLOT, HALF]])
                nc.vector.tensor_copy(pairs[:, t % 2, :, :], diag).then_inc(pairs_ready, 1)

            def pairs_turned(t):
                dve.wait_ge(pairsT_done, t + 1)
                if t >= 2:
                    dve.wait_ge(h1_done, t - 1)
                nc.vector.tensor_copy(pairsT[0:KP, t % 2, :, :],
                                      mix_ps[0:KP, 0:NKP * P].rearrange("p (c b) -> p c b", c=NKP)
                                      ).then_inc(pairsT_ready, 1)

            nc.vector.memset(featT[:, :, :, :, F:SLOT], 0.0).then_inc(pad_zero, 1)
            dve.wait_ge(tr_done, 1)
            for t in range(TILES):
                last = nc.vector.tensor_copy(featT[:, t, :, :, 0].rearrange("d q s -> d s q"),
                                             tr_ps[:, 0, t, :].rearrange("d (s q) -> d s q", s=NS))
            last.then_inc(tr_dve, 1)
            dve.wait_ge(w1d_in, 16)
            nc.vector.tensor_tensor(w1x[:, :], w1d_sb[:, 0, :], w1d_sb[:, 1, :], ALU.add).then_inc(w1x_ready, 1)
            for t in range(TILES):
                for g in range(NG):
                    if turn(t, g) % 2 == 0:
                        features(t, g)
                    if t >= 1 and g == 1:
                        pairs_turned(t - 1)
                for c in range(NCH):
                    diagonals(t, c)
                arrange_pairs(t)
            pairs_turned(TILES - 1)

        @block.tensor
        def _(pe):
            def stored(n):
                pe.wait_ge(tr_dve, dve_turns(n))
                pe.wait_ge(tr_act, 1 + act_turns(n))

            def turn_features(t, g):
                n = turn(t, g)
                pe.wait_ge(rows_in[t][g], 16 * len(groups[g]))
                if n == 2:
                    pe.wait_ge(tr_act, 1)
                if n >= 2:
                    if n % 2 == 0:
                        pe.wait_ge(tr_dve, dve_turns(n - 2))
                    else:
                        pe.wait_ge(tr_act, 1 + act_turns(n - 2))
                for i, f in enumerate(groups[g]):
                    last = nc.tensor.transpose(tr_ps[:, n % 2, i, :], rows[:, t, f, :], ident[:, :])
                last.then_inc(tr_done, 1)

            def gram_chunk(t, c):
                m = t * NCH + c
                if m >= 2:
                    pe.wait_ge(diag_act, m - 1)
                    pe.wait_ge(diag_dve, m - 1)
                for i in range(QC):
                    q = c * QC + i
                    four = featT[:, t, q, :, :]
                    dst = gram_ps[:, m % 2, i // QB, (i % QB) * NS * F:(i % QB + 1) * NS * F]
                    last = nc.tensor.matmul(dst.rearrange("p (s f) -> p s f", s=NS),
                                            four.rearrange("d s f -> d (s f)"), four[:, :, 0:F],
                                            start=True, stop=True)
                last.then_inc(gram_done, 1)

            def turn_pairs(t):
                pe.wait_ge(pairs_ready, t + 1)
                if t >= 1:
                    pe.wait_ge(h2_ready, t)
                flat = pairs[:, t % 2, :, :].rearrange("p f k -> p (f k)")
                for c in range(NKP):
                    last = nc.tensor.transpose(mix_ps[0:KP, c * P:(c + 1) * P], flat[:, c * KP:(c + 1) * KP],
                                               ident[:, :])
                last.then_inc(pairsT_done, 1)

            def layer1(t):
                pe.wait_ge(pairsT_ready, t + 1)
                if t == 0:
                    pe.wait_ge(w1x_ready, 1)
                    pe.wait_ge(w1p_in, 16)
                if t >= 1:
                    pe.wait_ge(y_ready, t)
                for j in range(J1):
                    cols = slice(j * P, (j + 1) * P)
                    nc.tensor.matmul(h1_ps[:, cols], w1x[:, cols], xT[:, t, :], start=True, stop=False)
                    for c in range(NKP):
                        last = nc.tensor.matmul(h1_ps[:, cols], w1p_sb[0:KP, c, cols], pairsT[0:KP, t % 2, c, :],
                                                start=False, stop=(c == NKP - 1))
                last.then_inc(h1_done, 1)

            def layer2(t):
                pe.wait_ge(h1_ready, t + 1)
                if t == 0:
                    pe.wait_ge(w2_in, 16)
                for j in range(J2):
                    cols = slice(j * P, (j + 1) * P)
                    for c in range(J1):
                        last = nc.tensor.matmul(mix_ps[:, cols], w2_sb[:, c, cols], h1T[:, t % 2, c, :],
                                                start=(c == 0), stop=(c == J1 - 1))
                last.then_inc(h2_done, 1)

            def layer3(t):
                pe.wait_ge(h2_ready, t + 1)
                if t == 0:
                    pe.wait_ge(par_in, 16)
                for c in range(J2):
                    last = nc.tensor.matmul(h1_ps[0:1, 0:P], par_sb[:, J1 + J2 + c:J1 + J2 + c + 1],
                                            h2T[:, t % 2, c, :], start=(c == 0), stop=(c == J2 - 1))
                last.then_inc(y_done, 1)

            pe.wait_ge(ident_ready, 1)
            pe.wait_ge(x_in, 16)
            for t in range(TILES):
                last = nc.tensor.transpose(tr_ps[:, 0, t, :], x_sb[:, t, :], ident[:, :])
            last.then_inc(tr_done, 1)
            pe.wait_ge(pad_zero, 1)
            for t in range(TILES):
                for g in range(NG):
                    turn_features(t, g)
                    if t >= 1:
                        if g == 0:
                            turn_pairs(t - 1)
                        if g == 2:
                            layer1(t - 1)
                        if g == 3:
                            layer2(t - 1)
                        if g == 4:
                            layer3(t - 1)
                stored(turn(t, NG - 1))
                for c in range(NCH):
                    gram_chunk(t, c)
            turn_pairs(TILES - 1)
            layer1(TILES - 1)
            layer2(TILES - 1)
            layer3(TILES - 1)


def kernel(**inputs):
    import numpy as np
    import concourse.bacc as bacc
    from concourse.bass_utils import run_bass_kernel_spmd

    P = 128
    NT = 26
    F = NT + 1
    HALF = (F - 1) // 2
    D = inputs["r_dense_features"].shape[1]
    w1 = np.asarray(inputs["W_top1"])
    H1 = w1.shape[1]
    H2 = inputs["W_top2"].shape[1]
    place = np.zeros((F, F), np.int64)
    iu, ju = np.triu_indices(F, k=1)
    place[iu, ju] = place[ju, iu] = D + np.arange(len(iu))
    order = np.array([place[f, (f + k) % F] for f in range(F) for k in range(1, HALF + 1)])
    KP = F * HALF // 3
    w1_pairs = w1[order].reshape(3, KP, H1).transpose(1, 0, 2)
    w1_dense = np.stack([w1[0:D], w1[D + len(iu):]], axis=1)
    w2 = np.asarray(inputs["W_top2"]).reshape(-1, P, H2).transpose(1, 0, 2)
    params = np.concatenate([np.asarray(inputs[k]).reshape(-1, P).T for k in ("b_top1", "b_top2", "W_top3")], axis=1)

    data = {"ids": inputs["ids"], "dense": inputs["r_dense_features"], "w1_pairs": w1_pairs,
            "w1_dense": w1_dense, "w2": w2, "params": params}
    data.update({f"tbl_{i}": inputs[f"tbl_{i}"] for i in range(NT)})
    nc = bacc.Bacc("TRN2", target_bir_lowering=False, num_devices=1)
    arrays, aps = {}, {}
    for name, a in data.items():
        a = np.ascontiguousarray(a)
        arrays[f"in_{name}"] = a
        aps[name] = nc.dram_tensor(f"in_{name}", a.shape, mybir.dt.from_np(a.dtype), kind="ExternalInput").ap()
    out = nc.dram_tensor("out_y", (inputs["ids"].shape[0], 1), F32, kind="ExternalOutput").ap()
    bass_dlrm_tower(nc, aps["ids"], aps["dense"], [aps[f"tbl_{i}"] for i in range(NT)],
                    aps["w1_pairs"], aps["w1_dense"], aps["w2"], aps["params"], out)
    r = run_bass_kernel_spmd(nc, [arrays], core_ids=[0])
    return r.results[0]["out_y"]
```

```python
from contextlib import ExitStack

import concourse.bass as bass
from concourse import mybir

F32 = mybir.dt.float32
F32R = mybir.dt.float32r
I32 = mybir.dt.int32
U32 = mybir.dt.uint32
ALU = mybir.AluOpType
ACT = mybir.ActivationFunctionType


def bass_dlrm_tower(nc, ids, dense, tables, small_ids, small_tables, w1_pairs, w1_dense, w2, params, out):
    P = 128
    B, D = dense.shape
    NT = len(tables)
    NL = len(small_tables)
    F = NT + NL + 1
    TILES = B // P
    SLOT = 32
    NS = P // SLOT
    NQ = P // NS
    HALF = (F - 1) // 2
    KP = w1_pairs.shape[0]
    NKP = w1_pairs.shape[1]
    H1 = w1_pairs.shape[2]
    H2 = w2.shape[2]
    J1, J2 = H1 // P, H2 // P
    GF = 4
    groups = [list(range(a, min(a + GF, NT))) for a in range(0, NT, GF)]
    NG = len(groups)
    QC = 8
    NCH = NQ // QC
    QB = 4
    KR = 125
    LK = [tbl.shape[0] // KR for tbl in small_tables]
    LKMAX = max(LK)
    RAW, OH = 3, 8
    assert all(k * KR == tbl.shape[0] for k, tbl in zip(LK, small_tables))

    def onehots_before(i):
        return sum(LK[:i])

    with ExitStack() as ctx:
        def sb(name, shape, dt=F32):
            return ctx.enter_context(nc.sbuf_tensor(name, shape, dt))

        def psum(name, shape):
            return ctx.enter_context(nc.psum_tensor(name, shape, F32))

        def sem(name):
            return ctx.enter_context(nc.semaphore(name))

        ids_sb = sb("ids_sb", [P, TILES, NT], I32)
        x_sb = sb("x_sb", [P, TILES, D])
        rows = sb("rows", [P, 2, NT, D])
        small_ids_sb = sb("small_ids_sb", [P, RAW, B], I32)
        table_sb = sb("table_sb", [P, RAW, LKMAX, D])
        table_hi = sb("table_hi", [P, 2, LKMAX, D], F32R)
        table_lo = sb("table_lo", [P, 2, LKMAX, D], F32R)
        onehot = sb("onehot", [P, OH, B], F32R)
        row_no_i = sb("row_no_i", [P, len(set(LK)), LKMAX], I32)
        row_no = sb("row_no", [P, len(set(LK)), LKMAX])
        ident = sb("ident", [P, P])
        featT = sb("featT", [P, TILES, NQ, NS, SLOT])
        xT = sb("xT", [P, TILES, P])
        gram = sb("gram", [P, 2, NQ, F])
        gramT = sb("gramT", [P, 2, F + HALF, SLOT])
        pairs = sb("pairs", [P, 2, F, HALF])
        pairsT = sb("pairsT", [P, 2, NKP, P])
        w1p_sb = sb("w1p_sb", [P, NKP, H1])
        w1d_sb = sb("w1d_sb", [P, 2, H1])
        w1x = sb("w1x", [P, H1])
        w2_sb = sb("w2_sb", [P, J1, H2])
        par_sb = sb("par_sb", [P, J1 + J2 + J2])
        h1T = sb("h1T", [P, 2, J1, P])
        h2T = sb("h2T", [P, 2, J2, P])
        y_sb = sb("y_sb", [1, P, TILES])

        tr_ps = psum("tr_ps", [P, 2, GF, P])
        gram_ps = psum("gram_ps", [P, 2, 2, 512])
        mlp_ps = psum("mlp_ps", [P, 2, 512])

        ids_in, x_in, w1p_in, w1d_in, w2_in, par_in = map(sem, (
            "ids_in", "x_in", "w1p_in", "w1d_in", "w2_in", "par_in"))
        rows_in = [[sem(f"rows_in_{t}_{g}") for g in range(NG)] for t in range(TILES)]
        ident_zero, ident_ready, pad_zero = sem("ident_zero"), sem("ident_ready"), sem("pad_zero")
        w1x_ready = sem("w1x_ready")
        table_in = [sem(f"table_in_{i}") for i in range(NL)]
        small_ids_in = [sem(f"small_ids_in_{i}") for i in range(NL)]
        iota_done, row_no_ready = sem("iota_done"), sem("row_no_ready")
        hi_ready, lo_ready, onehot_made = sem("hi_ready"), sem("lo_ready"), sem("onehot_made")
        onehot_used, lookup_stored = sem("onehot_used"), sem("lookup_stored")
        tr_done = sem("tr_done")
        dense_slot, tr_stored = sem("dense_slot"), sem("tr_stored")
        gram_done = sem("gram_done")
        diag_act, diag_dve = sem("diag_act"), sem("diag_dve")
        gramT_ready, pairs_ready = sem("gramT_ready"), sem("pairs_ready")
        pairsT_done, pairsT_ready = sem("pairsT_done"), sem("pairsT_ready")
        h1_done, h1_ready = sem("h1_done"), sem("h1_ready")
        h2_done, h2_ready = sem("h2_done"), sem("h2_ready")
        y_done, y_ready, y_out = sem("y_done"), sem("y_ready"), sem("y_out")

        def turn(t, g):
            return 1 + t * NG + g

        block = ctx.enter_context(nc.Block())

        @block.sync
        def _(sp):
            def small_table(i):
                if i >= RAW:
                    sp.wait_ge(onehot_made, onehots_before(i - RAW + 1))
                sp.dma_start(table_sb[0:KR, i % RAW, 0:LK[i], :],
                             small_tables[i].rearrange("(p k) d -> p k d", p=KR)).then_inc(table_in[i], 16)
                every = bass.AP(small_ids.tensor, small_ids[i:i + 1, :].offset, [[0, P], [1, B]])
                sp.dma_start(small_ids_sb[:, i % RAW, :], every).then_inc(small_ids_in[i], 16)

            sp.dma_start(ids_sb[:, :, :], ids.rearrange("(p t) f -> p t f", t=TILES)).then_inc(ids_in, 16)
            small_table(0)
            sp.dma_start(x_sb[:, :, :], dense.rearrange("(p t) d -> p t d", t=TILES)).then_inc(x_in, 16)
            for i in range(1, NL):
                small_table(i)
            sp.dma_start(par_sb[:, :], params).then_inc(par_in, 16)
            sp.dma_start(w1d_sb[:, :, :], w1_dense).then_inc(w1d_in, 16)
            sp.dma_start(w1p_sb[0:KP, :, :], w1_pairs).then_inc(w1p_in, 16)
            sp.dma_start(w2_sb[:, :, :], w2).then_inc(w2_in, 16)
            sp.wait_ge(y_ready, TILES)
            sp.dma_start(out.rearrange("(a p t) o -> a p (t o)", a=1, t=TILES), y_sb[:, :, :]).then_inc(y_out, 16)
            sp.wait_ge(y_out, 16)

        @block.gpsimd
        def _(pool):
            nc.gpsimd.memset(ident[:, :], 0.0).then_inc(ident_zero, 1)
            pool.wait_ge(ident_zero, 1)
            nc.gpsimd.affine_select(out=ident[:, :], in_=ident[:, :], compare_op=ALU.not_equal, fill=1.0,
                                    base=0, pattern=[[-1, P]], channel_multiplier=1).then_inc(ident_ready, 1)
            for m, n in enumerate(sorted(set(LK))):
                last = nc.gpsimd.iota(row_no_i[:, m, :], pattern=[[1, LKMAX]], base=0, channel_multiplier=n)
            last.then_inc(iota_done, 1)
            pool.wait_ge(ids_in, 16)
            for t in range(TILES):
                for g, fs in enumerate(groups):
                    if t >= 2:
                        pool.wait_ge(tr_done, turn(t - 2, g) + 1)
                    for f in fs:
                        pool.indirect_dma_start(
                            out=rows[:, t % 2, f, :], out_offset=None, in_=tables[f][:, :],
                            in_offset=bass.IndirectOffsetOnAxis(ap=ids_sb[:, t, f:f + 1].bitcast(U32), axis=0),
                        ).then_inc(rows_in[t][g], 16)

        def store_features(copy, t, g, n):
            fs = groups[g]
            src = tr_ps[:, n % 2, 0:len(fs), :].rearrange("d f (s q) -> d f s q", s=NS)
            dst = featT[:, t, :, :, 1 + fs[0]:2 + fs[-1]].rearrange("d q s f -> d f s q")
            return copy(dst, src)

        def store_diagonal(copy, t, c, s):
            src = gram_ps[SLOT * s:SLOT * (s + 1), (t * NCH + c) % 2, :, 0:QB * NS * F]
            src = src.rearrange("p b (q r g) -> p b q r g", q=QB, r=NS)[:, :, :, s, :]
            dst = gram[SLOT * s:SLOT * (s + 1), t % 2, c * QC:(c + 1) * QC, :]
            return copy(dst.rearrange("p (b q) g -> p b q g", q=QB), src)

        @block.scalar
        def _(act):
            def features(t, g):
                n = turn(t, g)
                act.wait_ge(tr_done, n + 1)
                store_features(nc.scalar.copy, t, g, n).then_inc(tr_stored, 1)

            def diagonals(t, c):
                act.wait_ge(gram_done, t * NCH + c + 1)
                if c == 0 and t >= 2:
                    act.wait_ge(gramT_ready, t - 1)
                for s in (0, 1):
                    last = store_diagonal(nc.scalar.copy, t, c, s)
                last.then_inc(diag_act, 1)

            def hidden1(t):
                if t >= 2:
                    act.wait_ge(h2_done, J2 * (t - 1))
                for j in range(J1):
                    act.wait_ge(h1_done, t * J1 + j + 1)
                    nc.scalar.activation(h1T[:, t % 2, j, :], mlp_ps[:, j % 2, (j // 2) * P:(j // 2 + 1) * P],
                                         ACT.Relu, bias=par_sb[:, j:j + 1]).then_inc(h1_ready, 1)

            def hidden2(t):
                if t >= 2:
                    act.wait_ge(y_done, t - 1)
                for j in range(J2):
                    act.wait_ge(h2_done, t * J2 + j + 1)
                    nc.scalar.activation(h2T[:, t % 2, j, :], mlp_ps[:, j, 0:P], ACT.Relu,
                                         bias=par_sb[:, J1 + j:J1 + j + 1]).then_inc(h2_ready, 1)

            def result(t):
                act.wait_ge(y_done, t + 1)
                nc.scalar.copy(y_sb[0:1, :, t], mlp_ps[0:1, 0, 0:P]).then_inc(y_ready, 1)

            def high_part(i):
                act.wait_ge(table_in[i], 16)
                if i >= 2:
                    act.wait_ge(onehot_used, onehots_before(i - 1))
                nc.scalar.copy(table_hi[0:KR, i % 2, 0:LK[i], :],
                               table_sb[0:KR, i % RAW, 0:LK[i], :]).then_inc(hi_ready, 1)

            def store_lookup(i):
                act.wait_ge(onehot_used, onehots_before(i + 1))
                dst = featT[:, :, :, :, 1 + NT + i].rearrange("d t q s -> d t s q")
                src = gram_ps[:, i % 2, 0, :].rearrange("d (t s q) -> d t s q", t=TILES, s=NS)
                nc.scalar.copy(dst, src).then_inc(lookup_stored, 1)

            high_part(0)
            act.wait_ge(tr_done, 1)
            act.wait_ge(dense_slot, 1)
            nc.scalar.copy(xT[:, :, :], tr_ps[:, 0, :, :]).then_inc(tr_stored, 1)
            for i in range(NL):
                if i + 1 < NL:
                    high_part(i + 1)
                store_lookup(i)
                features(i // NG, i % NG)
            for g in range(NG):
                if turn(0, g) > NL:
                    features(0, g)
            act.wait_ge(par_in, 16)
            for t in range(TILES):
                for c in range(NCH):
                    diagonals(t, c)
                    if t >= 1:
                        if c == 0:
                            hidden1(t - 1)
                        if c == 1:
                            hidden2(t - 1)
                        if c == 2:
                            result(t - 1)
                if t + 1 < TILES:
                    for g in range(NG):
                        if turn(t + 1, g) > NL:
                            features(t + 1, g)
            hidden1(TILES - 1)
            hidden2(TILES - 1)
            result(TILES - 1)

        @block.vector
        def _(dve):
            def diagonals(t, c):
                dve.wait_ge(gram_done, t * NCH + c + 1)
                for s in (2, 3):
                    last = store_diagonal(nc.vector.tensor_copy, t, c, s)
                last.then_inc(diag_dve, 1)

            def arrange_pairs(t):
                dve.wait_ge(diag_dve, NCH * (t + 1))
                dve.wait_ge(diag_act, NCH * (t + 1))
                src = gram[:, t % 2, :, :].rearrange("p q g -> p g q")
                nc.vector.transpose(gramT[:, t % 2, 0:F, :], src)
                nc.vector.transpose(gramT[:, t % 2, F:F + HALF, :], src[:, 0:HALF, :]).then_inc(gramT_ready, 1)
                dve.wait_ge(gramT_ready, t + 1)
                if t >= 2:
                    dve.wait_ge(pairsT_done, t - 1)
                flat = gramT[:, t % 2, :, :].rearrange("p g f -> p (g f)")
                diag = bass.AP(flat.tensor, flat.offset + SLOT, [list(flat.ap[0]), [SLOT + 1, F], [SLOT, HALF]])
                nc.vector.tensor_copy(pairs[:, t % 2, :, :], diag).then_inc(pairs_ready, 1)

            def pairs_turned(t):
                dve.wait_ge(pairsT_done, t + 1)
                if t >= 2:
                    dve.wait_ge(h1_done, J1 * (t - 1))
                nc.vector.tensor_copy(pairsT[0:KP, t % 2, :, :],
                                      mlp_ps[0:KP, 1, 0:NKP * P].rearrange("p (c b) -> p c b", c=NKP)
                                      ).then_inc(pairsT_ready, 1)

            def low_part(i):
                dve.wait_ge(hi_ready, i + 1)
                if i >= 2:
                    dve.wait_ge(onehot_used, onehots_before(i - 1))
                nc.vector.tensor_tensor(table_lo[0:KR, i % 2, 0:LK[i], :], table_sb[0:KR, i % RAW, 0:LK[i], :],
                                        table_hi[0:KR, i % 2, 0:LK[i], :].bitcast(F32),
                                        ALU.subtract).then_inc(lo_ready, 1)

            def onehots(i):
                dve.wait_ge(small_ids_in[i], 16)
                kind = sorted(set(LK)).index(LK[i])
                for k in range(LK[i]):
                    n = onehots_before(i) + k
                    if n >= OH:
                        dve.wait_ge(onehot_used, n - OH + 1)
                    nc.vector.tensor_scalar(onehot[0:KR, n % OH, :], small_ids_sb[0:KR, i % RAW, :],
                                            row_no[0:KR, kind, k:k + 1], None,
                                            ALU.is_equal).then_inc(onehot_made, 1)

            nc.vector.memset(featT[:, :, :, :, F:SLOT], 0.0).then_inc(pad_zero, 1)
            dve.wait_ge(iota_done, 1)
            nc.vector.tensor_copy(row_no[:, :, :], row_no_i[:, :, :]).then_inc(row_no_ready, 1)
            dve.wait_ge(row_no_ready, 1)
            dve.wait_ge(tr_done, 1)
            nc.vector.tensor_copy(featT[:, :, :, :, 0].rearrange("d t q s -> d t s q"),
                                  tr_ps[:, 0, :, :].rearrange("d t (s q) -> d t s q", s=NS)).then_inc(dense_slot, 1)
            for i in range(NL):
                low_part(i)
                onehots(i)
            dve.wait_ge(w1d_in, 16)
            nc.vector.tensor_tensor(w1x[:, :], w1d_sb[:, 0, :], w1d_sb[:, 1, :], ALU.add).then_inc(w1x_ready, 1)
            for t in range(TILES):
                for c in range(NCH):
                    diagonals(t, c)
                arrange_pairs(t)
                pairs_turned(t)

        @block.tensor
        def _(pe):
            def turn_features(t, g):
                n = turn(t, g)
                pe.wait_ge(rows_in[t][g], 16 * len(groups[g]))
                if n >= 2:
                    pe.wait_ge(tr_stored, n - 1)
                for i, f in enumerate(groups[g]):
                    last = nc.tensor.transpose(tr_ps[:, n % 2, i, :], rows[:, t % 2, f, :], ident[:, :])
                last.then_inc(tr_done, 1)

            def gram_chunk(t, c):
                m = t * NCH + c
                if m >= 2:
                    pe.wait_ge(diag_act, m - 1)
                    pe.wait_ge(diag_dve, m - 1)
                for i in range(QC):
                    q = c * QC + i
                    four = featT[:, t, q, :, :]
                    dst = gram_ps[:, m % 2, i // QB, (i % QB) * NS * F:(i % QB + 1) * NS * F]
                    last = nc.tensor.matmul(dst.rearrange("p (s f) -> p s f", s=NS),
                                            four.rearrange("d s f -> d (s f)"), four[:, :, 0:F],
                                            start=True, stop=True)
                last.then_inc(gram_done, 1)

            def turn_pairs(t):
                pe.wait_ge(pairs_ready, t + 1)
                if t >= 1:
                    pe.wait_ge(h2_ready, J2 * t)
                flat = pairs[:, t % 2, :, :].rearrange("p f k -> p (f k)")
                for c in range(NKP):
                    last = nc.tensor.transpose(mlp_ps[0:KP, 1, c * P:(c + 1) * P], flat[:, c * KP:(c + 1) * KP],
                                               ident[:, :])
                last.then_inc(pairsT_done, 1)

            def layer1(t):
                pe.wait_ge(pairsT_ready, t + 1)
                if t >= 1:
                    pe.wait_ge(y_ready, t)
                for j in range(J1):
                    cols = slice(j * P, (j + 1) * P)
                    if j >= 2:
                        pe.wait_ge(h1_ready, t * J1 + j - 1)
                    dst = mlp_ps[:, j % 2, (j // 2) * P:(j // 2 + 1) * P]
                    nc.tensor.matmul(dst, w1x[:, cols], xT[:, t, :], start=True, stop=False)
                    for c in range(NKP):
                        last = nc.tensor.matmul(dst, w1p_sb[0:KP, c, cols], pairsT[0:KP, t % 2, c, :],
                                                start=False, stop=(c == NKP - 1))
                    last.then_inc(h1_done, 1)

            def layer2(t):
                for j in range(J2):
                    for c in range(J1):
                        if j == 0:
                            pe.wait_ge(h1_ready, t * J1 + max(c + 1, J1 - 1))
                        else:
                            pe.wait_ge(h1_ready, (t + 1) * J1)
                        last = nc.tensor.matmul(mlp_ps[:, j, 0:P], w2_sb[:, c, j * P:(j + 1) * P],
                                                h1T[:, t % 2, c, :], start=(c == 0), stop=(c == J1 - 1))
                    last.then_inc(h2_done, 1)

            def layer3(t):
                for c in range(J2):
                    pe.wait_ge(h2_ready, t * J2 + c + 1)
                    last = nc.tensor.matmul(mlp_ps[0:1, 0, 0:P], par_sb[:, J1 + J2 + c:J1 + J2 + c + 1],
                                            h2T[:, t % 2, c, :], start=(c == 0), stop=(c == J2 - 1))
                last.then_inc(y_done, 1)

            def lookup(i):
                if i >= 2:
                    pe.wait_ge(lookup_stored, i - 1)
                pe.wait_ge(lo_ready, i + 1)
                for k in range(LK[i]):
                    n = onehots_before(i) + k
                    pe.wait_ge(onehot_made, n + 1)
                    nc.tensor.matmul(gram_ps[:, i % 2, 0, :], table_hi[0:KR, i % 2, k, :], onehot[0:KR, n % OH, :],
                                     start=(k == 0), stop=False)
                    nc.tensor.matmul(gram_ps[:, i % 2, 0, :], table_lo[0:KR, i % 2, k, :], onehot[0:KR, n % OH, :],
                                     start=False, stop=(k == LK[i] - 1)).then_inc(onehot_used, 1)

            pe.wait_ge(ident_ready, 1)
            pe.wait_ge(x_in, 16)
            for t in range(TILES):
                last = nc.tensor.transpose(tr_ps[:, 0, t, :], x_sb[:, t, :], ident[:, :])
            last.then_inc(tr_done, 1)
            for i in range(NL):
                lookup(i)
                turn_features(i // NG, i % NG)
            for g in range(NG):
                if turn(0, g) > NL:
                    turn_features(0, g)
            pe.wait_ge(pad_zero, 1)
            pe.wait_ge(lookup_stored, NL)
            pe.wait_ge(w1x_ready, 1)
            pe.wait_ge(w1p_in, 16)
            pe.wait_ge(w2_in, 16)
            pe.wait_ge(par_in, 16)
            for t in range(TILES):
                pe.wait_ge(tr_stored, turn(t, NG - 1) + 1)
                for c in range(NCH):
                    gram_chunk(t, c)
                    if t >= 1:
                        if c == 0:
                            layer1(t - 1)
                        if c == 1:
                            layer2(t - 1)
                        if c == 2:
                            layer3(t - 1)
                if t + 1 < TILES:
                    for g in range(NG):
                        if turn(t + 1, g) > NL:
                            turn_features(t + 1, g)
                turn_pairs(t)
            layer1(TILES - 1)
            layer2(TILES - 1)
            layer3(TILES - 1)


def kernel(**inputs):
    import numpy as np
    import concourse.bacc as bacc
    from concourse.bass_utils import run_bass_kernel_spmd

    P = 128
    NT = 26
    SMALL = 8
    F = NT + 1
    HALF = (F - 1) // 2
    D = inputs["r_dense_features"].shape[1]
    w1 = np.asarray(inputs["W_top1"])
    H1 = w1.shape[1]
    H2 = inputs["W_top2"].shape[1]
    by_size = sorted(range(NT), key=lambda f: inputs[f"tbl_{f}"].shape[0])
    small, large = sorted(by_size[:SMALL]), sorted(by_size[SMALL:])
    slots = [0] + [1 + f for f in large + small]
    place = np.zeros((F, F), np.int64)
    iu, ju = np.triu_indices(F, k=1)
    place[iu, ju] = place[ju, iu] = D + np.arange(len(iu))
    order = np.array([place[slots[f], slots[(f + k) % F]] for f in range(F) for k in range(1, HALF + 1)])
    KP = F * HALF // 3
    w1_pairs = w1[order].reshape(3, KP, H1).transpose(1, 0, 2)
    w1_dense = np.stack([w1[0:D], w1[D + len(iu):]], axis=1)
    w2 = np.asarray(inputs["W_top2"]).reshape(-1, P, H2).transpose(1, 0, 2)
    params = np.concatenate([np.asarray(inputs[k]).reshape(-1, P).T for k in ("b_top1", "b_top2", "W_top3")], axis=1)

    ids = np.asarray(inputs["ids"])
    B = ids.shape[0]
    small_ids = ids[:, small].reshape(P, B // P, SMALL).transpose(2, 1, 0).reshape(SMALL, B)
    data = {"ids": ids[:, large], "small_ids": small_ids, "dense": inputs["r_dense_features"], "w1_pairs": w1_pairs,
            "w1_dense": w1_dense, "w2": w2, "params": params}
    data.update({f"tbl_{i}": inputs[f"tbl_{i}"] for i in range(NT)})
    nc = bacc.Bacc("TRN2", target_bir_lowering=False, num_devices=1)
    arrays, aps = {}, {}
    for name, a in data.items():
        a = np.ascontiguousarray(a)
        arrays[f"in_{name}"] = a
        aps[name] = nc.dram_tensor(f"in_{name}", a.shape, mybir.dt.from_np(a.dtype), kind="ExternalInput").ap()
    out = nc.dram_tensor("out_y", (B, 1), F32, kind="ExternalOutput").ap()
    bass_dlrm_tower(nc, aps["ids"], aps["dense"], [aps[f"tbl_{i}"] for i in large],
                    aps["small_ids"], [aps[f"tbl_{i}"] for i in small], aps["w1_pairs"], aps["w1_dense"], aps["w2"], aps["params"], out)
    r = run_bass_kernel_spmd(nc, [arrays], core_ids=[0])
    return r.results[0]["out_y"]
```

```python
from contextlib import ExitStack

import concourse.bass as bass
from concourse import mybir

F32 = mybir.dt.float32
F32R = mybir.dt.float32r
I32 = mybir.dt.int32
U32 = mybir.dt.uint32
ALU = mybir.AluOpType
ACT = mybir.ActivationFunctionType


def bass_dlrm_tower(nc, ids, dense, tables, small_ids, small_tables, w1_pairs, w1_dense, w2, params, out):
    P = 128
    B, D = dense.shape
    NT = len(tables)
    NL = len(small_tables)
    F = NT + NL + 1
    TILES = B // P
    SLOT = 32
    NS = P // SLOT
    NQ = P // NS
    HALF = (F - 1) // 2
    KP = w1_pairs.shape[0]
    NKP = w1_pairs.shape[1]
    H1 = w1_pairs.shape[2]
    H2 = w2.shape[2]
    J1, J2 = H1 // P, H2 // P
    GF = 4
    groups = [list(range(a, min(a + GF, NT))) for a in range(0, NT, GF)]
    NG = len(groups)
    QC = 8
    QB = 4
    NCH = NQ // QC
    KR = 125
    LK = [tbl.shape[0] // KR for tbl in small_tables]
    LKMAX = max(LK)
    RAW, OH = 3, 8
    WARM = 14
    assert LK[0] - 1 <= OH
    assert all(k * KR == tbl.shape[0] for k, tbl in zip(LK, small_tables))

    def onehots_before(i):
        return sum(k - 1 for k in LK[:i])

    with ExitStack() as ctx:
        def sb(name, shape, dt=F32):
            return ctx.enter_context(nc.sbuf_tensor(name, shape, dt))

        def psum(name, shape):
            return ctx.enter_context(nc.psum_tensor(name, shape, F32))

        def sem(name):
            return ctx.enter_context(nc.semaphore(name))

        ids_sb = sb("ids_sb", [P, TILES, NT], I32)
        x_sb = sb("x_sb", [P, TILES, D])
        rows = sb("rows", [P, 2, NT, D])
        small_ids_sb = sb("small_ids_sb", [P, RAW, B], I32)
        table_sb = sb("table_sb", [P, RAW, LKMAX, D])
        table_hi = sb("table_hi", [P, 2, LKMAX, D], F32R)
        table_lo = sb("table_lo", [P, 2, LKMAX, D], F32R)
        onehot = sb("onehot", [P, OH, B], F32R)
        distance = sb("distance", [P, B])
        onehot_act = sb("onehot_act", [P, 2, B], F32R)
        neg_row_no = sb("neg_row_no", [P, len(set(LK)), LKMAX])
        one = sb("one", [P, 1])
        row_no_i = sb("row_no_i", [P, len(set(LK)), LKMAX], I32)
        row_no = sb("row_no", [P, len(set(LK)), LKMAX])
        ident = sb("ident", [P, P])
        featT = sb("featT", [P, TILES, NQ, NS, SLOT])
        xT = sb("xT", [P, TILES, P])
        gram = sb("gram", [P, 2, NQ, F])
        gramT = sb("gramT", [P, 2, F + HALF, SLOT])
        pairs = sb("pairs", [P, 2, F, HALF])
        pairsT = sb("pairsT", [P, 2, NKP, P])
        w1p_sb = sb("w1p_sb", [P, NKP, H1])
        w1d_sb = sb("w1d_sb", [P, 2, H1])
        w1x = sb("w1x", [P, H1])
        w2_sb = sb("w2_sb", [P, J1, H2])
        par_sb = sb("par_sb", [P, J1 + J2 + J2])
        h1T = sb("h1T", [P, 2, J1, P])
        h2T = sb("h2T", [P, 2, J2, P])
        y_sb = sb("y_sb", [1, P, TILES])

        tr_ps = psum("tr_ps", [P, 2, GF, P])
        gram_ps = psum("gram_ps", [P, 2, 2, 512])
        mlp_ps = psum("mlp_ps", [P, 2, 512])

        ids_in, x_in, w1p_in, w1d_in, w2_in, par_in = map(sem, (
            "ids_in", "x_in", "w1p_in", "w1d_in", "w2_in", "par_in"))
        rows_in = [[sem(f"rows_in_{t}_{g}") for g in range(NG)] for t in range(TILES)]
        ident_zero, ident_ready, pad_zero = sem("ident_zero"), sem("ident_ready"), sem("pad_zero")
        w1x_ready = sem("w1x_ready")
        table_in = [sem(f"table_in_{i}") for i in range(NL)]
        small_ids_in = [sem(f"small_ids_in_{i}") for i in range(NL)]
        iota_done, row_no_ready = sem("iota_done"), sem("row_no_ready")
        hi_ready, lo_ready, onehot_made = sem("hi_ready"), sem("lo_ready"), sem("onehot_made")
        one_ready, distance_made, act_onehot_made = sem("one_ready"), sem("distance_made"), sem("act_onehot_made")
        onehot_used, lookup_stored = sem("onehot_used"), sem("lookup_stored")
        tr_done, tr_stored = sem("tr_done"), sem("tr_stored")
        gram_done = sem("gram_done")
        diag_act, diag_dve = sem("diag_act"), sem("diag_dve")
        gramT_ready, pairs_ready = sem("gramT_ready"), sem("pairs_ready")
        pairsT_done, pairsT_ready = sem("pairsT_done"), sem("pairsT_ready")
        h1_done, h1_ready = sem("h1_done"), sem("h1_ready")
        h2_done, h2_ready = sem("h2_done"), sem("h2_ready")
        y_done, y_ready, y_out = sem("y_done"), sem("y_ready"), sem("y_out")

        LAST = TILES - 1

        def h1_block(t, j):
            if t == LAST:
                return (tr_ps[:, 0, 0, :], tr_ps[:, 1, 0, :], gram_ps[:, 0, 0, 0:P], gram_ps[:, 0, 1, 0:P])[j]
            return mlp_ps[:, j % 2, (j // 2) * P:(j // 2 + 1) * P]

        def pairs_block(t, c):
            if t == LAST:
                return (mlp_ps[0:KP, 1, 0:P], gram_ps[0:KP, 1, 0, 0:P], gram_ps[0:KP, 1, 1, 0:P])[c]
            return mlp_ps[0:KP, 1, c * P:(c + 1) * P]

        def turn(t, g):
            return 1 + t * NG + g

        slot_ends = {LAST - 2: (NG - 2, NG - 2, NG, NG), LAST - 1: (1, NG - 2, NG - 1, NG)}

        def turns_in(t, slot):
            ends = (0,) + slot_ends.get(t, (NG, NG, NG, NG))
            return [g for g in range(ends[slot], ends[slot + 1]) if t < LAST and turn(t + 1, g) > NL]

        block = ctx.enter_context(nc.Block())

        @block.sync
        def _(sp):
            def small_table(i):
                if i >= RAW:
                    sp.wait_ge(lo_ready, i - RAW + 1)
                    sp.wait_ge(onehot_made, onehots_before(i - RAW + 1))
                    sp.wait_ge(act_onehot_made, i - RAW + 1)
                every = bass.AP(small_ids.tensor, small_ids[i:i + 1, :].offset, [[0, P], [1, B]])
                sp.dma_start(small_ids_sb[:, i % RAW, :], every).then_inc(small_ids_in[i], 16)
                src = small_tables[i].rearrange("(p k) d -> p k d", p=KR)
                for part in (slice(0, KR // 16 * 16), slice(KR // 16 * 16, KR)):
                    sp.dma_start(table_sb[part, i % RAW, 0:LK[i], :], src[part]).then_inc(table_in[i], 16)

            sp.dma_start(ids_sb[:, :, :], ids.rearrange("(p t) f -> p t f", t=TILES)).then_inc(ids_in, 16)
            small_table(0)
            small_table(1)
            sp.dma_start(x_sb[:, :, :], dense.rearrange("(p t) d -> p t d", t=TILES)).then_inc(x_in, 16)
            for i in range(2, NL):
                small_table(i)
            sp.dma_start(par_sb[:, :], params).then_inc(par_in, 16)
            sp.dma_start(w1d_sb[:, :, :], w1_dense).then_inc(w1d_in, 16)
            sp.dma_start(w1p_sb[0:KP, :, :], w1_pairs).then_inc(w1p_in, 16)
            sp.dma_start(w2_sb[:, :, :], w2).then_inc(w2_in, 16)
            sp.wait_ge(y_ready, TILES)
            sp.dma_start(out.rearrange("(a p t) o -> a p (t o)", a=1, t=TILES), y_sb[:, :, :]).then_inc(y_out, 16)
            sp.wait_ge(y_out, 16)

        @block.gpsimd
        def _(pool):
            nc.gpsimd.memset(ident[:, :], 0.0).then_inc(ident_zero, 1)
            pool.wait_ge(ident_zero, 1)
            nc.gpsimd.affine_select(out=ident[:, :], in_=ident[:, :], compare_op=ALU.not_equal, fill=1.0,
                                    base=0, pattern=[[-1, P]], channel_multiplier=1).then_inc(ident_ready, 1)
            for m, n in enumerate(sorted(set(LK))):
                last = nc.gpsimd.iota(row_no_i[:, m, :], pattern=[[1, LKMAX]], base=0, channel_multiplier=n)
            last.then_inc(iota_done, 1)
            pool.wait_ge(ids_in, 16)
            for t in range(TILES):
                for g, fs in enumerate(groups):
                    if t >= 2:
                        pool.wait_ge(tr_done, turn(t - 2, g) + 1)
                    for f in fs:
                        pool.indirect_dma_start(
                            out=rows[:, t % 2, f, :], out_offset=None, in_=tables[f][:, :],
                            in_offset=bass.IndirectOffsetOnAxis(ap=ids_sb[:, t, f:f + 1].bitcast(U32), axis=0),
                        ).then_inc(rows_in[t][g], 16)

        def store_features(copy, t, g, n):
            fs = groups[g]
            src = tr_ps[:, n % 2, 0:len(fs), :].rearrange("d f (s q) -> d f s q", s=NS)
            dst = featT[:, t, :, :, 1 + fs[0]:2 + fs[-1]].rearrange("d q s f -> d f s q")
            return copy(dst, src)

        def store_diagonal(copy, t, c, s):
            src = gram_ps[SLOT * s:SLOT * (s + 1), (t * NCH + c) % 2, :, 0:QB * NS * F]
            src = src.rearrange("p b (q r g) -> p b q r g", q=QB, r=NS)[:, :, :, s, :]
            dst = gram[SLOT * s:SLOT * (s + 1), t % 2, c * QC:(c + 1) * QC, :]
            return copy(dst.rearrange("p (b q) g -> p b q g", q=QB), src)

        @block.scalar
        def _(act):
            def features(t, g):
                n = turn(t, g)
                act.wait_ge(tr_done, n + 1)
                store_features(nc.scalar.copy, t, g, n).then_inc(tr_stored, 1)

            def diagonals(t, c):
                act.wait_ge(gram_done, t * NCH + c + 1)
                if c == 0 and t >= 2:
                    act.wait_ge(gramT_ready, 2 * (t - 1))
                for s in (0, 1):
                    last = store_diagonal(nc.scalar.copy, t, c, s)
                last.then_inc(diag_act, 1)

            def hidden1(t):
                if t >= 2:
                    act.wait_ge(h2_done, J2 * (t - 1))
                for j in range(J1):
                    act.wait_ge(h1_done, t * J1 + j + 1)
                    nc.scalar.activation(h1T[:, t % 2, j, :], h1_block(t, j), ACT.Relu,
                                         bias=par_sb[:, j:j + 1]).then_inc(h1_ready, 1)

            def hidden2(t):
                if t >= 2:
                    act.wait_ge(y_done, t - 1)
                for j in range(J2):
                    act.wait_ge(h2_done, t * J2 + j + 1)
                    nc.scalar.activation(h2T[:, t % 2, j, :], mlp_ps[:, j, 0:P], ACT.Relu,
                                         bias=par_sb[:, J1 + j:J1 + j + 1]).then_inc(h2_ready, 1)

            def result(t):
                act.wait_ge(y_done, t + 1)
                nc.scalar.copy(y_sb[0:1, :, t], mlp_ps[0:1, 0, 0:P]).then_inc(y_ready, 1)

            def high_part(i):
                act.wait_ge(table_in[i], 32)
                if i >= 2:
                    act.wait_ge(onehot_used, onehots_before(i - 1))
                half = LK[i] // 2
                for ks in (slice(0, half), slice(half, LK[i])):
                    nc.scalar.copy(table_hi[0:KR, i % 2, ks, :],
                                   table_sb[0:KR, i % RAW, ks, :]).then_inc(hi_ready, 1)

            def last_onehot(i):
                act.wait_ge(small_ids_in[i], 16)
                k, kind = LK[i] - 1, sorted(set(LK)).index(LK[i])
                if i == 0:
                    act.wait_ge(row_no_ready, 2)
                    act.wait_ge(one_ready, 1)
                else:
                    act.wait_ge(act_onehot_made, i)
                nc.scalar.activation(distance[0:KR, :], small_ids_sb[0:KR, i % RAW, :], ACT.Abs,
                                     bias=neg_row_no[0:KR, kind, k:k + 1]).then_inc(distance_made, 1)
                act.wait_ge(distance_made, i + 1)
                nc.scalar.activation(onehot_act[0:KR, i % 2, :], distance[0:KR, :], ACT.Relu, scale=-1.0,
                                     bias=one[0:KR, :]).then_inc(act_onehot_made, 1)

            def store_lookup(i):
                act.wait_ge(onehot_used, onehots_before(i + 1))
                dst = featT[:, :, :, :, 1 + NT + i].rearrange("d t q s -> d t s q")
                src = gram_ps[:, i % 2, 0, :].rearrange("d (t s q) -> d t s q", t=TILES, s=NS)
                nc.scalar.copy(dst, src).then_inc(lookup_stored, 1)

            high_part(0)
            last_onehot(0)
            for i in range(NL):
                if i + 1 < NL:
                    high_part(i + 1)
                    last_onehot(i + 1)
                store_lookup(i)
                if i == 0:
                    act.wait_ge(tr_done, 1)
                    nc.scalar.copy(featT[:, :, :, :, 0].rearrange("d t q s -> d t s q"),
                                   tr_ps[:, 0, :, :].rearrange("d t (s q) -> d t s q", s=NS))
                    nc.scalar.copy(xT[:, :, :], tr_ps[:, 0, :, :]).then_inc(tr_stored, 1)
                if i > 0:
                    features((i - 1) // NG, (i - 1) % NG)
            features((NL - 1) // NG, (NL - 1) % NG)
            for g in range(NG):
                if turn(0, g) > NL:
                    features(0, g)
            act.wait_ge(par_in, 16)
            for t in range(TILES):
                for c in range(NCH - 1):
                    diagonals(t, c)
                if 1 <= t < LAST:
                    hidden1(t - 1)
                for g in turns_in(t, 0):
                    features(t + 1, g)
                diagonals(t, NCH - 1)
                for g in turns_in(t, 1):
                    features(t + 1, g)
                if t >= 1:
                    hidden2(t - 1)
                for g in turns_in(t, 2):
                    features(t + 1, g)
                if t >= 1:
                    result(t - 1)
                for g in turns_in(t, 3):
                    features(t + 1, g)
                if t == LAST - 1:
                    hidden1(t)
            hidden1(LAST)
            hidden2(LAST)
            result(LAST)

        @block.vector
        def _(dve):
            def diagonals(t, c):
                dve.wait_ge(gram_done, t * NCH + c + 1)
                for s in (2, 3):
                    last = store_diagonal(nc.vector.tensor_copy, t, c, s)
                last.then_inc(diag_dve, 1)

            def arrange_pairs(t):
                dve.wait_ge(diag_dve, NCH * (t + 1))
                dve.wait_ge(diag_act, NCH * (t + 1))
                src = gram[:, t % 2, :, :].rearrange("p q g -> p g q")
                nc.vector.transpose(gramT[:, t % 2, 0:F, :], src).then_inc(gramT_ready, 1)
                dve.wait_ge(gramT_ready, 2 * t + 1)
                if t >= 2:
                    dve.wait_ge(pairsT_done, NKP * (t - 1))
                flat = gramT[:, t % 2, :, :].rearrange("p g f -> p (g f)")
                FC = F // NKP
                for c in range(NKP):
                    if c > 0:
                        dve.wait_ge(gramT_ready, 2 * t + 2)
                    diag = bass.AP(flat.tensor, flat.offset + SLOT + c * FC * (SLOT + 1),
                                   [list(flat.ap[0]), [SLOT + 1, FC], [SLOT, HALF]])
                    nc.vector.tensor_copy(pairs[:, t % 2, c * FC:(c + 1) * FC, :], diag).then_inc(pairs_ready, 1)
                    if c == 0:
                        nc.vector.transpose(gramT[:, t % 2, F:F + HALF, :], src[:, 0:HALF, :]).then_inc(gramT_ready, 1)

            def pairs_turned(t):
                if t >= 2:
                    dve.wait_ge(h1_done, J1 * (t - 1))
                for c in range(NKP):
                    dve.wait_ge(pairsT_done, NKP * t + (c + 1 if t == LAST else NKP))
                    nc.vector.tensor_copy(pairsT[0:KP, t % 2, c, :], pairs_block(t, c)).then_inc(pairsT_ready, 1)

            def low_part(i):
                dve.wait_ge(hi_ready, 2 * (i + 1))
                if i >= 2:
                    dve.wait_ge(onehot_used, onehots_before(i - 1))
                nc.vector.tensor_tensor(table_lo[0:KR, i % 2, 0:LK[i], :], table_sb[0:KR, i % RAW, 0:LK[i], :],
                                        table_hi[0:KR, i % 2, 0:LK[i], :].bitcast(F32),
                                        ALU.subtract).then_inc(lo_ready, 1)

            def onehots(i):
                dve.wait_ge(small_ids_in[i], 16)
                kind = sorted(set(LK)).index(LK[i])
                for k in range(LK[i] - 1):
                    n = onehots_before(i) + k
                    if n >= OH:
                        dve.wait_ge(onehot_used, n - OH + 1)
                    nc.vector.tensor_scalar(onehot[0:KR, n % OH, :], small_ids_sb[0:KR, i % RAW, :],
                                            row_no[0:KR, kind, k:k + 1], None,
                                            ALU.is_equal).then_inc(onehot_made, 1)

            nc.vector.memset(one[:, :], 1.0).then_inc(one_ready, 1)
            nc.vector.memset(featT[:, :, :, :, F:SLOT], 0.0).then_inc(pad_zero, 1)
            dve.wait_ge(iota_done, 1)
            nc.vector.tensor_copy(row_no[:, :, :], row_no_i[:, :, :]).then_inc(row_no_ready, 1)
            nc.vector.tensor_scalar(neg_row_no[:, :, :], row_no_i[:, :, :], -1.0, None,
                                    ALU.mult).then_inc(row_no_ready, 1)
            dve.wait_ge(row_no_ready, 1)
            onehots(0)
            low_part(0)
            for i in range(1, NL):
                low_part(i)
                onehots(i)
            dve.wait_ge(w1d_in, 16)
            nc.vector.tensor_tensor(w1x[:, :], w1d_sb[:, 0, :], w1d_sb[:, 1, :], ALU.add).then_inc(w1x_ready, 1)
            for t in range(TILES):
                for c in range(NCH):
                    diagonals(t, c)
                    if 1 <= t < LAST and c == 1:
                        pairs_turned(t - 1)
                arrange_pairs(t)
                if t >= LAST - 1:
                    pairs_turned(t)

        @block.tensor
        def _(pe):
            def turn_features(t, g):
                n = turn(t, g)
                pe.wait_ge(rows_in[t][g], 16 * len(groups[g]))
                if n >= 2:
                    pe.wait_ge(tr_stored, n - 1)
                for i, f in enumerate(groups[g]):
                    last = nc.tensor.transpose(tr_ps[:, n % 2, i, :], rows[:, t % 2, f, :], ident[:, :])
                last.then_inc(tr_done, 1)

            def gram_chunk(t, c):
                m = t * NCH + c
                if m >= 2:
                    pe.wait_ge(diag_act, m - 1)
                    pe.wait_ge(diag_dve, m - 1)
                for i in range(QC):
                    q = c * QC + i
                    four = featT[:, t, q, :, :]
                    dst = gram_ps[:, m % 2, i // QB, (i % QB) * NS * F:(i % QB + 1) * NS * F]
                    last = nc.tensor.matmul(dst.rearrange("p (s f) -> p s f", s=NS),
                                            four.rearrange("d s f -> d (s f)"), four[:, :, 0:F],
                                            start=True, stop=True)
                last.then_inc(gram_done, 1)

            def turn_pairs(t):
                if t >= 1:
                    pe.wait_ge(h2_ready, J2 * t)
                flat = pairs[:, t % 2, :, :].rearrange("p f k -> p (f k)")
                for c in range(NKP):
                    pe.wait_ge(pairs_ready, NKP * t + c + 1)
                    nc.tensor.transpose(pairs_block(t, c), flat[:, c * KP:(c + 1) * KP],
                                        ident[:, :]).then_inc(pairsT_done, 1)

            def layer1_dense(t, j):
                nc.tensor.matmul(h1_block(t, j), w1x[:, j * P:(j + 1) * P], xT[:, t, :], start=True, stop=False)

            def layer1_pairs(t, j, c):
                last = nc.tensor.matmul(h1_block(t, j), w1p_sb[0:KP, c, j * P:(j + 1) * P],
                                        pairsT[0:KP, t % 2, c, :], start=False, stop=(c == NKP - 1))
                if c == NKP - 1:
                    last.then_inc(h1_done, 1)

            def layer1(t):
                pe.wait_ge(pairsT_ready, NKP * (t + 1))
                if t >= 1:
                    pe.wait_ge(y_ready, t)
                for j in range(J1):
                    if j >= 2:
                        pe.wait_ge(h1_ready, t * J1 + j - 1)
                    layer1_dense(t, j)
                    for c in range(NKP):
                        layer1_pairs(t, j, c)

            def layer1_last(t):
                for c in range(NKP):
                    pe.wait_ge(pairsT_ready, NKP * t + c + 1)
                    for j in range(J1):
                        layer1_pairs(t, j, c)

            def layer2_product(t, j, c):
                last = nc.tensor.matmul(mlp_ps[:, j, 0:P], w2_sb[:, c, j * P:(j + 1) * P],
                                        h1T[:, t % 2, c, :], start=(c == 0), stop=(c == J1 - 1))
                if c == J1 - 1:
                    last.then_inc(h2_done, 1)

            def layer2(t):
                for j in range(J2):
                    pe.wait_ge(h1_ready, t * J1 + J1 - 1 + j)
                    for c in range(J1):
                        if j == 0 and c == J1 - 1:
                            pe.wait_ge(h1_ready, (t + 1) * J1)
                        layer2_product(t, j, c)

            def layer2_last(t):
                pe.wait_ge(y_ready, t)
                for c in range(J1):
                    pe.wait_ge(h1_ready, t * J1 + c + 1)
                    for j in range(J2):
                        layer2_product(t, j, c)

            def layer3(t):
                for c in range(J2):
                    pe.wait_ge(h2_ready, t * J2 + c + 1)
                    last = nc.tensor.matmul(mlp_ps[0:1, 0, 0:P], par_sb[:, J1 + J2 + c:J1 + J2 + c + 1],
                                            h2T[:, t % 2, c, :], start=(c == 0), stop=(c == J2 - 1))
                last.then_inc(y_done, 1)

            def lookup(i):
                if i >= 2:
                    pe.wait_ge(lookup_stored, i - 1)
                pe.wait_ge(hi_ready, 2 * i + 1 if i == 0 else 2 * (i + 1))
                bank = gram_ps[:, i % 2, 0, :]
                last_k = LK[i] - 1

                def product(part, k, rows_of_k, start=False, stop=False):
                    return nc.tensor.matmul(bank, part[0:KR, i % 2, k, :], rows_of_k[0:KR], start=start, stop=stop)

                def made_by_dve(k):
                    n = onehots_before(i) + k
                    pe.wait_ge(onehot_made, n + 1)
                    return onehot[:, n % OH, :]

                def made_by_act():
                    pe.wait_ge(act_onehot_made, i + 1)
                    return onehot_act[:, i % 2, :]

                if i == 0:
                    for k in range(last_k):
                        if k == LK[0] // 2:
                            pe.wait_ge(hi_ready, 2)
                        product(table_hi, k, made_by_dve(k), start=(k == 0))
                    product(table_hi, last_k, made_by_act())
                    pe.wait_ge(lo_ready, 1)
                    product(table_lo, last_k, made_by_act())
                else:
                    product(table_hi, last_k, made_by_act(), start=True)
                    pe.wait_ge(lo_ready, i + 1)
                    product(table_lo, last_k, made_by_act())
                for k in range(last_k):
                    if i > 0:
                        product(table_hi, k, made_by_dve(k))
                    product(table_lo, k, made_by_dve(k), stop=(k == last_k - 1)).then_inc(onehot_used, 1)

            pe.wait_ge(ident_ready, 1)
            for i in range(WARM):
                nc.tensor.matmul(gram_ps[:, 1, 1, 0:P], ident[:, :], ident[:, :], start=True, stop=True)
            for i in range(NL):
                lookup(i)
                if i == 0:
                    pe.wait_ge(x_in, 16)
                    for t in range(TILES):
                        last = nc.tensor.transpose(tr_ps[:, 0, t, :], x_sb[:, t, :], ident[:, :])
                    last.then_inc(tr_done, 1)
                if i > 0:
                    turn_features((i - 1) // NG, (i - 1) % NG)
            turn_features((NL - 1) // NG, (NL - 1) % NG)
            for g in range(NG):
                if turn(0, g) > NL:
                    turn_features(0, g)
            pe.wait_ge(pad_zero, 1)
            pe.wait_ge(lookup_stored, NL)
            pe.wait_ge(w1x_ready, 1)
            pe.wait_ge(w1p_in, 16)
            pe.wait_ge(w2_in, 16)
            pe.wait_ge(par_in, 16)
            for t in range(TILES):
                pe.wait_ge(tr_stored, turn(t, NG - 1) + 1)
                gram_chunk(t, 0)
                gram_chunk(t, 1)
                if 1 <= t < LAST:
                    turn_pairs(t - 1)
                for c in range(2, NCH - 1):
                    gram_chunk(t, c)
                if 1 <= t < LAST:
                    layer1(t - 1)
                for g in turns_in(t, 0):
                    turn_features(t + 1, g)
                gram_chunk(t, NCH - 1)
                for g in turns_in(t, 1):
                    turn_features(t + 1, g)
                if t >= 1:
                    layer2(t - 1)
                for g in turns_in(t, 2):
                    turn_features(t + 1, g)
                if t == LAST:
                    pe.wait_ge(diag_act, NCH * TILES - 1)
                    pe.wait_ge(diag_dve, NCH * TILES - 1)
                    for j in range(J1):
                        layer1_dense(LAST, j)
                    turn_pairs(LAST)
                if t >= 1:
                    layer3(t - 1)
                if t == LAST - 1:
                    turn_pairs(t)
                for g in turns_in(t, 3):
                    turn_features(t + 1, g)
                if t == LAST - 1:
                    layer1(t)
            layer1_last(LAST)
            layer2_last(LAST)
            layer3(LAST)


def kernel(**inputs):
    import numpy as np
    import concourse.bacc as bacc
    from concourse.bass_utils import run_bass_kernel_spmd

    P = 128
    NT = 26
    SMALL = 8
    F = NT + 1
    HALF = (F - 1) // 2
    D = inputs["r_dense_features"].shape[1]
    w1 = np.asarray(inputs["W_top1"])
    H1 = w1.shape[1]
    H2 = inputs["W_top2"].shape[1]
    by_size = sorted(range(NT), key=lambda f: inputs[f"tbl_{f}"].shape[0])
    small, large = sorted(by_size[:SMALL]), sorted(by_size[SMALL:])
    slots = [0] + [1 + f for f in large + small]
    place = np.zeros((F, F), np.int64)
    iu, ju = np.triu_indices(F, k=1)
    place[iu, ju] = place[ju, iu] = D + np.arange(len(iu))
    order = np.array([place[slots[f], slots[(f + k) % F]] for f in range(F) for k in range(1, HALF + 1)])
    KP = F * HALF // 3
    w1_pairs = w1[order].reshape(3, KP, H1).transpose(1, 0, 2)
    w1_dense = np.stack([w1[0:D], w1[D + len(iu):]], axis=1)
    w2 = np.asarray(inputs["W_top2"]).reshape(-1, P, H2).transpose(1, 0, 2)
    params = np.concatenate([np.asarray(inputs[k]).reshape(-1, P).T for k in ("b_top1", "b_top2", "W_top3")], axis=1)

    ids = np.asarray(inputs["ids"])
    B = ids.shape[0]
    small_ids = ids[:, small].reshape(P, B // P, SMALL).transpose(2, 1, 0).reshape(SMALL, B)
    data = {"ids": ids[:, large], "small_ids": small_ids, "dense": inputs["r_dense_features"], "w1_pairs": w1_pairs,
            "w1_dense": w1_dense, "w2": w2, "params": params}
    data.update({f"tbl_{i}": inputs[f"tbl_{i}"] for i in range(NT)})
    nc = bacc.Bacc("TRN2", target_bir_lowering=False, num_devices=1)
    arrays, aps = {}, {}
    for name, a in data.items():
        a = np.ascontiguousarray(a)
        arrays[f"in_{name}"] = a
        aps[name] = nc.dram_tensor(f"in_{name}", a.shape, mybir.dt.from_np(a.dtype), kind="ExternalInput").ap()
    out = nc.dram_tensor("out_y", (B, 1), F32, kind="ExternalOutput").ap()
    bass_dlrm_tower(nc, aps["ids"], aps["dense"], [aps[f"tbl_{i}"] for i in large],
                    aps["small_ids"], [aps[f"tbl_{i}"] for i in small],
                    aps["w1_pairs"], aps["w1_dense"], aps["w2"], aps["params"], out)
    r = run_bass_kernel_spmd(nc, [arrays], core_ids=[0])
    return r.results[0]["out_y"]
```
